# Optimizing a Trainium2 kernel written in Bass

```python
import numpy as np
import jax
import jax.numpy as jnp

def _softmax(x, axis=-1):
    return jax.nn.softmax(x, axis=axis)

def _gelu(x):
    return jax.nn.gelu(x, approximate=True)

def _silu(x):
    return jax.nn.silu(x)

def _sigmoid(x):
    return jax.nn.sigmoid(x)

def _layernorm(x, axis=-1, eps=1e-05):
    m = jnp.mean(x, axis=axis, keepdims=True)
    v = jnp.var(x, axis=axis, keepdims=True)
    return (x - m) / jnp.sqrt(v + eps)

def _scatter_add(tgt, idx, src, axis=0):
    return tgt.at[idx].add(src)

def _segment_sum(src, seg, n):
    return jax.ops.segment_sum(src, seg, n)
kernel_name = 'mk_rec_standalone_d1_rec_r8_748985'

def setup_inputs(seed: int=0):
    np.random.seed(seed)
    _w = jnp.asarray

    def _rec_inputs():
        import jax
        import jax.numpy as jnp
        _rk = jax.random.key(seed)
        r_movie_id = jax.random.randint(jax.random.fold_in(_rk, 1), (2048, 1), 145, 999883, jnp.int32)
        r_target_movie_id = jax.random.randint(jax.random.fold_in(_rk, 2), (2048, 1), 238, 999973, jnp.int32)
        return (r_movie_id, r_target_movie_id)
    r_movie_id, r_target_movie_id = _rec_inputs()

    def _L0_rec_setup():
        import jax, jax.numpy as jnp
        import numpy as np
        VOCAB = 125000
        EMBED = 64
        BATCH = 1024
        NUM_SAMPLED = 1024
        NEG_INF = -1000000000.0

        def _log_uniform_expected_count(ids, num_sampled, range_max):
            idsf = ids.astype(jnp.float32)
            p = (jnp.log(idsf + 2.0) - jnp.log(idsf + 1.0)) / jnp.log(float(range_max) + 1.0)
            return -jnp.expm1(num_sampled * jnp.log1p(-p))
        key = jax.random.key(seed)
        k1, k2, k3, k4, k5, k6 = jax.random.split(key, 6)
        movie_id = jax.random.randint(k1, (BATCH, 1), 0, VOCAB, dtype=jnp.int32)
        target_movie_id = jax.random.randint(k2, (BATCH, 1), 0, VOCAB, dtype=jnp.int32)
        sampled_ids = jax.random.randint(k3, (NUM_SAMPLED,), 0, VOCAB, dtype=jnp.int32)
        front_emb = jax.random.normal(k4, (VOCAB, EMBED), dtype=jnp.float32) * 0.05
        after_emb = jax.random.normal(k5, (VOCAB, EMBED), dtype=jnp.float32) * 0.05
        after_bias = jax.random.normal(k6, (VOCAB,), dtype=jnp.float32) * 0.05
        return {'movie_id': movie_id, 'target_movie_id': target_movie_id, 'sampled_ids': sampled_ids, 'front_emb': front_emb, 'after_emb': after_emb, 'after_bias': after_bias}
    _L0_rec_all = _L0_rec_setup()
    _L0_rec_in = {k: v for k, v in _L0_rec_all.items() if k in ('sampled_ids', 'front_emb', 'after_emb', 'after_bias')}
    del _L0_rec_all
    return {'r_movie_id': r_movie_id, 'r_target_movie_id': r_target_movie_id, 'L0_rec_sampled_ids': _L0_rec_in['sampled_ids'], 'L0_rec_front_emb': _L0_rec_in['front_emb'], 'L0_rec_after_emb': _L0_rec_in['after_emb'], 'L0_rec_after_bias': _L0_rec_in['after_bias']}

def reference(r_movie_id, r_target_movie_id, L0_rec_sampled_ids, L0_rec_front_emb, L0_rec_after_emb, L0_rec_after_bias):
    import jax
    import jax.numpy as jnp

    def _L0_rec_ref(movie_id, target_movie_id, sampled_ids, front_emb, after_emb, after_bias):
        import jax, jax.numpy as jnp
        import numpy as np
        VOCAB = 125000
        EMBED = 64
        BATCH = 1024
        NUM_SAMPLED = 1024
        NEG_INF = -1000000000.0

        def _log_uniform_expected_count(ids, num_sampled, range_max):
            idsf = ids.astype(jnp.float32)
            p = (jnp.log(idsf + 2.0) - jnp.log(idsf + 1.0)) / jnp.log(float(range_max) + 1.0)
            return -jnp.expm1(num_sampled * jnp.log1p(-p))
        inputs = front_emb[movie_id[:, 0]]
        labels = target_movie_id[:, 0]
        true_w = after_emb[labels]
        true_b = after_bias[labels]
        samp_w = after_emb[sampled_ids]
        samp_b = after_bias[sampled_ids]
        true_logits = jnp.sum(inputs * true_w, axis=-1) + true_b
        sampled_logits = jnp.einsum('bd,sd->bs', inputs, samp_w) + samp_b
        true_logits = true_logits - jnp.log(_log_uniform_expected_count(labels, NUM_SAMPLED, VOCAB))
        sampled_logits = sampled_logits - jnp.log(_log_uniform_expected_count(sampled_ids, NUM_SAMPLED, VOCAB))[None, :]
        hits = sampled_ids[None, :] == labels[:, None]
        sampled_logits = jnp.where(hits, sampled_logits + NEG_INF, sampled_logits)
        logits = jnp.concatenate([true_logits[:, None], sampled_logits], axis=1)
        loss = jax.nn.logsumexp(logits, axis=1) - logits[:, 0]
        return loss
    y = _L0_rec_ref(r_movie_id, r_target_movie_id, L0_rec_sampled_ids, L0_rec_front_emb, L0_rec_after_emb, L0_rec_after_bias)
    return y

_drawn_inputs = setup_inputs


def setup_inputs(seed=0):
    import zlib

    import numpy as np

    out = dict(_drawn_inputs(seed))
    spreads = {}
    factors = {'L0_rec_front_emb': 8.0, 'L0_rec_after_emb': 8.0, 'L0_rec_after_bias': 7.005}
    for name, (base, spread) in spreads.items():
        noise = np.random.default_rng([zlib.crc32(name.encode()), seed]).standard_normal(out[name].shape)
        drawn = base * np.exp(spread * noise) if base else spread * noise
        out[name] = jnp.asarray(drawn.astype(out[name].dtype))
    for name, factor in factors.items():
        out[name] = (out[name] * factor).astype(out[name].dtype)
    return out
```

```python
import math

import numpy as np
import concourse.bass as bass
from concourse import mybir
from concourse.alu_op_type import AluOpType as ALU
from contextlib import ExitStack

P = 128
VOCAB = 125000
EMBED = 64
AUG = EMBED + 1
SAMPLES = 1024
BATCH = 2048
SAMPLE_TILES = SAMPLES // P
TILES = BATCH // P
NEG_INF = -1e9
SLOTS = 4
GROUP = 4
BANK = 512
CORR = SAMPLE_TILES + TILES

SQRT_HALF = 0.70710677
LOG_P = (0.070376836, -0.1151461, 0.116769984)
LOG_Q = (-0.12420141, 0.14249323, -0.16668057)
LOG_R = (0.20000714, -0.24999994, 0.3333333)
LN2_LOW, LN2_HIGH = -0.00021219444, 0.6933594


def log_uniform_loss(nc, ids, sample_row, front, after, out):
    f32, i32 = mybir.dt.float32, mybir.dt.int32
    ACT = mybir.ActivationFunctionType
    AX = mybir.AxisListType
    ctx = ExitStack()
    with ctx:
        def sb(name, shape, dt=f32):
            return ctx.enter_context(nc.sbuf_tensor(name, shape, dt))

        def sem(name):
            return ctx.enter_context(nc.semaphore(name))

        LAB = SAMPLE_TILES
        MOV = SAMPLE_TILES + TILES
        COLS = MOV + TILES
        id_cols = sb("id_cols", [P, COLS], i32)
        wrap = sb("wrap", [P, COLS])
        wrapped = sb("wrapped", [P, COLS])
        rows = sb("rows", [P, COLS], i32)
        label = sb("label", [P, TILES])
        neg_label = sb("neg_label", [P, TILES])
        sample_ids = sb("sample_ids", [P, SAMPLES], i32)
        ident = sb("ident", [P, P])
        neg_inf = sb("neg_inf", [P, 1])
        ln_big = sb("ln_big", [P, 1])

        w_rows = sb("w_rows", [P, SAMPLE_TILES, AUG])
        x_rows = sb("x_rows", [P, TILES, AUG])
        t_rows = sb("t_rows", [P, TILES, AUG])
        wT = sb("wT", [AUG, SAMPLES])
        xT = sb("xT", [AUG, 2, P])
        masks = sb("masks", [P, TILES, SAMPLES])
        prod = sb("prod", [P, TILES, AUG])

        x12 = sb("x12", [P, 2 * CORR])
        expo = sb("expo", [P, 2 * CORR], i32)
        mant_i = sb("mant_i", [P, 2 * CORR], i32)
        small = sb("small", [P, 2 * CORR])
        expf = sb("expf", [P, 2 * CORR])
        mk = sb("mk", [P, 2 * CORR])
        r = sb("r", [P, 2 * CORR])
        r2 = sb("r2", [P, 2 * CORR])
        r3 = sb("r3", [P, 2 * CORR])
        pa = sb("pa", [P, 2 * CORR])
        pq = sb("pq", [P, 2 * CORR])
        pr = sb("pr", [P, 2 * CORR])
        half = sb("half", [P, 2 * CORR])
        logs = sb("logs", [P, 2 * CORR])
        diff = sb("diff", [P, CORR])
        tt = sb("tt", [P, CORR])
        ser = sb("ser", [P, CORR])
        et = sb("et", [P, CORR])
        quot = sb("quot", [P, CORR])
        sel = sb("sel", [P, CORR], i32)
        neg_id = sb("neg_id", [P, CORR])
        log_count = sb("log_count", [P, CORR])

        row_max = sb("row_max", [P, 2, TILES])
        neg_max = sb("neg_max", [P, TILES])
        sums = sb("sums", [P, TILES])
        dots = sb("dots", [P, TILES])
        top = sb("top", [P, TILES])
        shifted = sb("shifted", [P, 2, TILES])
        weights = sb("weights", [P, 2, TILES])
        total = sb("total", [P, TILES])
        log_total = sb("log_total", [P, TILES])
        loss = sb("loss", [P, TILES])

        logits = ctx.enter_context(nc.psum_tensor("logits", [P, SLOTS, SAMPLES], f32))

        ids_in = sem("ids_in")
        row_in = sem("row_in")
        rows_ok = sem("rows_ok")
        consts_ok = sem("consts_ok")
        ident_step = sem("ident_step")
        ident_ok = sem("ident_ok")
        labels_ok = sem("labels_ok")
        w_in = sem("w_in")
        x_in = [sem(f"x_in{k}") for k in range(GROUP)]
        t_in = [sem(f"t_in{k}") for k in range(GROUP)]
        step = sem("step")
        t_ready = sem("t_ready")
        et_ok = sem("et_ok")
        quot_ok = sem("quot_ok")
        log_count_ok = sem("log_count_ok")
        w_ok = sem("w_ok")
        w_turned = sem("w_turned")
        wT_ok = sem("wT_ok")
        x_turned = sem("x_turned")
        x_copied = sem("x_copied")
        logits_ok = sem("logits_ok")
        act_mask = sem("act_mask")
        act_square = sem("act_square")
        dve_mask = sem("dve_mask")
        max_ok = sem("max_ok")
        neg_ok = sem("neg_ok")
        exp_ok = sem("exp_ok")
        dot_ok = sem("dot_ok")
        shifted_ok = sem("shifted_ok")
        weights_ok = sem("weights_ok")
        total_ok = sem("total_ok")
        log_ok = sem("log_ok")
        loss_ok = sem("loss_ok")
        out_ok = sem("out_ok")

        on_act = lambda t: t % 4 < 2
        act_masks = [t for t in range(TILES) if on_act(t)]
        dve_masks = [t for t in range(TILES) if not on_act(t)]

        block = ctx.enter_context(nc.Block())

        @block.sync
        def _(sp):
            sp.dma_start(id_cols[:, :], ids).then_inc(ids_in, 16)
            sp.dma_start(sample_ids[:, :], sample_row.rearrange("(a n) -> a n", a=1).to_broadcast([P, SAMPLES])).then_inc(row_in, 16)
            sp.wait_ge(loss_ok, 1)
            sp.dma_start(out.rearrange("(p t) -> p t", t=TILES), loss[:, :]).then_inc(out_ok, 16)
            sp.wait_ge(out_ok, 16)

        @block.gpsimd
        def _(pool):
            pool.memset(ident[:, :], 0.0).then_inc(ident_step, 1)
            pool.memset(x_rows[:, :, EMBED], 1.0).then_inc(consts_ok, 1)
            pool.wait_ge(ident_step, 1)
            pool.affine_select(out=ident[:, :], in_=ident[:, :], compare_op=ALU.not_equal, fill=1.0,
                               base=0, pattern=[[-1, P]], channel_multiplier=1).then_inc(ident_ok, 1)

            def gather(dst, table, col):
                return pool.indirect_dma_start(dst, None, table,
                                               bass.IndirectOffsetOnAxis(ap=rows[:, col:col + 1], axis=0))

            pool.wait_ge(rows_ok, 1)
            for j in range(SAMPLE_TILES):
                gather(w_rows[:, j, :], after, j).then_inc(w_in, 16)
            for t in range(TILES):
                g, k = divmod(t, GROUP)
                if g:
                    pool.wait_ge(x_in[k], 16 * g)
                    pool.wait_ge(t_in[k], 16 * g)
                gather(x_rows[:, t, 0:EMBED], front, MOV + t).then_inc(x_in[k], 16)
                gather(t_rows[:, t, :], after, LAB + t).then_inc(t_in[k], 16)

        @block.tensor
        def _(pe):
            pe.wait_ge(ident_ok, 1)
            pe.wait_ge(consts_ok, 1)

            def turn_x(t):
                g, k = divmod(t, GROUP)
                pe.wait_ge(x_in[k], 16 * (g + 1))
                if t >= SLOTS:
                    pe.wait_ge(exp_ok, t - SLOTS + 1)
                nc.tensor.transpose(logits[0:AUG, t % SLOTS, 0:P], x_rows[:, t, :], ident[:, :]).then_inc(x_turned, 1)

            pe.wait_ge(w_ok, 1)
            for j in range(SAMPLE_TILES):
                m = nc.tensor.transpose(logits[0:AUG, SLOTS - 1, j * P:(j + 1) * P], w_rows[:, j, :], ident[:, :])
                if j % 4 == 3:
                    m.then_inc(w_turned, 1)
            turn_x(0)
            pe.wait_ge(wT_ok, 2)
            for t in range(TILES):
                if t + 1 < TILES:
                    turn_x(t + 1)
                pe.wait_ge(x_copied, t + 1)
                for h in range(2):
                    m = nc.tensor.matmul(logits[:, t % SLOTS, h * BANK:(h + 1) * BANK], xT[:, t % 2, :],
                                         wT[:, h * BANK:(h + 1) * BANK], start=True, stop=True)
                m.then_inc(logits_ok, 1)

        @block.scalar
        def _(act):
            nc.scalar.preload_act_table_set("natural_log_exp_and_others")
            made = [0]

            def square(t):
                nc.scalar.activation(masks[:, t, :], sample_ids[:, :], ACT.Square,
                                     bias=neg_label[:, t:t + 1], scale=1.0).then_inc(act_square, 1)

            def hit(t):
                made[0] += 1
                act.wait_ge(act_square, made[0])
                nc.scalar.activation(masks[:, t, :], masks[:, t, :], ACT.Exp, bias=ln_big[:, 0:1],
                                     scale=-256.0).then_inc(act_mask, 1)

            act.wait_ge(row_in, 16)
            act.wait_ge(labels_ok, 1)
            square(act_masks[0])
            square(act_masks[1])
            hit(act_masks[0])
            act.wait_ge(t_ready, 1)
            nc.scalar.activation(et[:, :], tt[:, :], ACT.Exp, scale=-1.0).then_inc(et_ok, 1)
            hit(act_masks[1])
            square(act_masks[2])
            act.wait_ge(quot_ok, 1)
            nc.scalar.activation(log_count[:, :], quot[:, :], ACT.Ln).then_inc(log_count_ok, 1)
            hit(act_masks[2])
            square(act_masks[3])
            hit(act_masks[3])
            todo = list(act_masks[4:])
            act.wait_ge(w_turned, 1)
            nc.scalar.copy(wT[:, 0:BANK], logits[0:AUG, SLOTS - 1, 0:BANK]).then_inc(wT_ok, 1)

            def copy_x(t):
                act.wait_ge(x_turned, t + 1)
                if t >= 2:
                    act.wait_ge(logits_ok, t - 1)
                nc.scalar.copy(xT[:, t % 2, :], logits[0:AUG, t % SLOTS, 0:P]).then_inc(x_copied, 1)

            copy_x(0)
            for t in range(TILES):
                if t + 1 < TILES:
                    copy_x(t + 1)
                act.wait_ge(max_ok, t + 1)
                nc.scalar.activation(logits[:, t % SLOTS, :], logits[:, t % SLOTS, :], ACT.Exp, bias=neg_max[:, t:t + 1],
                                     accum_out=sums[:, t:t + 1]).then_inc(exp_ok, 1)
                if todo:
                    if t % 2 == 0:
                        square(todo[0])
                    else:
                        hit(todo.pop(0))
            act.wait_ge(shifted_ok, 1)
            nc.scalar.activation(weights[:, :, :], shifted[:, :, :], ACT.Exp).then_inc(weights_ok, 1)
            act.wait_ge(total_ok, 1)
            nc.scalar.activation(log_total[:, :], total[:, :], ACT.Ln).then_inc(log_ok, 1)

        @block.vector
        def _(dve):
            done = [0]
            V = nc.vector

            def link(ins):
                done[0] += 1
                ins.then_inc(step, 1)
                dve.wait_ge(step, done[0])

            dve.wait_ge(ids_in, 16)
            link(V.tensor_scalar(wrap[:, :], id_cols[:, :], 0.0, float(VOCAB), ALU.is_lt, ALU.mult))
            link(V.scalar_tensor_tensor(wrapped[:, :], id_cols[:, :], float(VOCAB - 1), wrap[:, :], ALU.min, ALU.add))
            V.tensor_scalar(rows[:, :], wrapped[:, :], 0.0, None, ALU.max).then_inc(rows_ok, 1)
            V.memset(neg_inf[:, :], -NEG_INF)
            V.memset(ln_big[:, :], math.log(-NEG_INF))
            V.tensor_scalar(label[:, :], id_cols[:, LAB:MOV], 1.0, None, ALU.mult)
            link(V.tensor_scalar(neg_label[:, :], id_cols[:, LAB:MOV], -1.0, None, ALU.mult))
            V.tensor_scalar(neg_id[:, :], id_cols[:, 0:CORR], 0.0, 3e38, ALU.min, ALU.mult).then_inc(labels_ok, 1)

            V.tensor_scalar(x12[:, 0:CORR], id_cols[:, 0:CORR], 1.0, None, ALU.add)
            link(V.tensor_scalar(x12[:, CORR:], id_cols[:, 0:CORR], 2.0, None, ALU.add))
            bits = x12[:, :].bitcast(i32)
            V.tensor_scalar(expo[:, :], bits, 23, None, ALU.logical_shift_right)
            link(V.tensor_scalar(mant_i[:, :], bits, 0x7fffff, 0x3f000000, ALU.bitwise_and, ALU.bitwise_or))
            m = mant_i[:, :].bitcast(f32)
            V.tensor_scalar(small[:, :], m, SQRT_HALF, None, ALU.is_lt)
            link(V.scalar_tensor_tensor(mk[:, :], m, SQRT_HALF, m, ALU.is_lt, ALU.mult))
            V.scalar_tensor_tensor(expf[:, :], expo[:, :], 126.0, small[:, :], ALU.subtract, ALU.subtract)
            link(V.scalar_tensor_tensor(r[:, :], m, 1.0, mk[:, :], ALU.subtract, ALU.add))
            V.tensor_scalar(pa[:, :], r[:, :], LOG_P[0], LOG_P[1], ALU.mult, ALU.add)
            V.tensor_scalar(pq[:, :], r[:, :], LOG_Q[0], LOG_Q[1], ALU.mult, ALU.add)
            V.tensor_scalar(pr[:, :], r[:, :], LOG_R[0], LOG_R[1], ALU.mult, ALU.add)
            link(V.tensor_tensor(r2[:, :], r[:, :], r[:, :], ALU.mult))
            V.tensor_tensor(pa[:, :], pa[:, :], r[:, :], ALU.mult)
            V.tensor_tensor(pq[:, :], pq[:, :], r[:, :], ALU.mult)
            V.tensor_tensor(pr[:, :], pr[:, :], r[:, :], ALU.mult)
            V.scalar_tensor_tensor(half[:, :], r2[:, :], -0.5, r[:, :], ALU.mult, ALU.add)
            link(V.tensor_tensor(r3[:, :], r2[:, :], r[:, :], ALU.mult))
            link(V.scalar_tensor_tensor(pa[:, :], pa[:, :], LOG_P[2], r3[:, :], ALU.add, ALU.mult))
            link(V.scalar_tensor_tensor(pa[:, :], pq[:, :], LOG_Q[2], pa[:, :], ALU.add, ALU.add))
            link(V.tensor_tensor(pa[:, :], pa[:, :], r3[:, :], ALU.mult))
            link(V.scalar_tensor_tensor(pa[:, :], pr[:, :], LOG_R[2], pa[:, :], ALU.add, ALU.add))
            link(V.tensor_tensor(pa[:, :], pa[:, :], r3[:, :], ALU.mult))
            link(V.scalar_tensor_tensor(pa[:, :], expf[:, :], LN2_LOW, pa[:, :], ALU.mult, ALU.add))
            link(V.tensor_tensor(half[:, :], half[:, :], pa[:, :], ALU.add))
            link(V.scalar_tensor_tensor(logs[:, :], expf[:, :], LN2_HIGH, half[:, :], ALU.mult, ALU.add))
            link(V.tensor_tensor(diff[:, :], logs[:, CORR:], logs[:, 0:CORR], ALU.subtract))

            log_range = math.log(VOCAB + 1.0)
            c = [SAMPLES / (n * log_range ** n) for n in range(1, 7)]
            link(V.tensor_scalar(tt[:, :], diff[:, :], c[5], c[4], ALU.mult, ALU.add))
            link(V.tensor_tensor(tt[:, :], tt[:, :], diff[:, :], ALU.mult))
            for n in (3, 2, 1):
                link(V.scalar_tensor_tensor(tt[:, :], tt[:, :], c[n], diff[:, :], ALU.add, ALU.mult))
            link(V.scalar_tensor_tensor(tt[:, :], tt[:, :], c[0], diff[:, :], ALU.add, ALU.mult))
            e = [(-1.0) ** n / math.factorial(n + 1) for n in range(8)]
            V.tensor_scalar(sel[:, :], tt[:, :], 0.5, None, ALU.is_lt).then_inc(t_ready, 1)
            link(V.tensor_scalar(ser[:, :], tt[:, :], e[7], e[6], ALU.mult, ALU.add))
            link(V.tensor_tensor(ser[:, :], ser[:, :], tt[:, :], ALU.mult))
            for n in (5, 4, 3, 2, 1, 0):
                link(V.scalar_tensor_tensor(ser[:, :], ser[:, :], e[n], tt[:, :], ALU.add, ALU.mult))
            dve.wait_ge(et_ok, 1)
            link(V.tensor_scalar(quot[:, :], et[:, :], -1.0, 1.0, ALU.mult, ALU.add))
            link(V.copy_predicated(quot[:, :], sel[:, :], ser[:, :]))
            V.tensor_tensor(quot[:, :], quot[:, :], neg_id[:, :], ALU.add).then_inc(quot_ok, 1)

            todo = list(dve_masks)

            def make_mask():
                if todo:
                    t = todo.pop(0)
                    V.scalar_tensor_tensor(masks[:, t, :], sample_ids[:, :], label[:, t:t + 1],
                                           neg_inf[:, 0:1].to_broadcast([P, SAMPLES]), ALU.is_equal,
                                           ALU.mult).then_inc(dve_mask, 1)

            dve.wait_ge(row_in, 16)
            for _ in range(3):
                make_mask()
            dve.wait_ge(log_count_ok, 1)
            dve.wait_ge(w_in, 16 * SAMPLE_TILES)
            V.tensor_tensor(w_rows[:, :, EMBED], w_rows[:, :, EMBED], log_count[:, 0:SAMPLE_TILES],
                            ALU.subtract).then_inc(w_ok, 1)
            dve.wait_ge(w_turned, 2)
            V.tensor_copy(wT[:, BANK:], logits[0:AUG, SLOTS - 1, BANK:]).then_inc(wT_ok, 1)
            dve.wait_ge(consts_ok, 1)

            def top_logit(t):
                dve.wait_ge(logits_ok, t + 1)
                if on_act(t):
                    dve.wait_ge(act_mask, act_masks.index(t) + 1)
                else:
                    dve.wait_ge(dve_mask, dve_masks.index(t) + 1)
                V.tensor_tensor_reduce(out=logits[:, t % SLOTS, :], in0=logits[:, t % SLOTS, :], in1=masks[:, t, :],
                                       scale=1.0, scalar=-3e38, op0=ALU.subtract, op1=ALU.max,
                                       accum_out=row_max[:, 0, t:t + 1]).then_inc(neg_ok, 1)

            def negate(t):
                dve.wait_ge(neg_ok, t + 1)
                V.tensor_scalar(neg_max[:, t:t + 1], row_max[:, 0, t:t + 1], -1.0, None, ALU.mult).then_inc(max_ok, 1)

            def dot(t):
                g, k = divmod(t, GROUP)
                dve.wait_ge(x_in[k], 16 * (g + 1))
                dve.wait_ge(t_in[k], 16 * (g + 1))
                V.tensor_tensor_reduce(out=prod[:, t, :], in0=x_rows[:, t, :], in1=t_rows[:, t, :],
                                       scale=1.0, scalar=0.0, op0=ALU.mult, op1=ALU.add,
                                       accum_out=dots[:, t:t + 1]).then_inc(dot_ok, 1)

            for t in range(TILES):
                top_logit(t)
                negate(t)
                make_mask()
                if t >= 2:
                    if t > 2:
                        dve.wait_ge(dot_ok, t - 2)
                    dot(t - 2)
            for t in (TILES - 2, TILES - 1):
                dve.wait_ge(dot_ok, t)
                dot(t)
            dve.wait_ge(dot_ok, TILES)
            link(V.tensor_tensor(row_max[:, 1, :], dots[:, :], log_count[:, SAMPLE_TILES:], ALU.subtract))
            link(V.tensor_tensor(top[:, :], row_max[:, 0, :], row_max[:, 1, :], ALU.max))
            V.tensor_tensor(shifted[:, 0, :], row_max[:, 0, :], top[:, :], ALU.subtract)
            V.tensor_tensor(shifted[:, 1, :], row_max[:, 1, :], top[:, :], ALU.subtract).then_inc(shifted_ok, 1)
            dve.wait_ge(weights_ok, 1)
            dve.wait_ge(exp_ok, TILES)
            link(V.tensor_tensor(total[:, :], sums[:, :], weights[:, 0, :], ALU.mult))
            V.tensor_tensor(total[:, :], total[:, :], weights[:, 1, :], ALU.add).then_inc(total_ok, 1)
            dve.wait_ge(log_ok, 1)
            V.tensor_tensor(loss[:, :], log_total[:, :], shifted[:, 1, :], ALU.subtract).then_inc(loss_ok, 1)


def kernel(**inputs):
    import concourse.bacc as bacc
    from concourse.bass_utils import run_bass_kernel_spmd as run

    nc = bacc.Bacc("TRN2", target_bir_lowering=False, num_devices=1)
    got = {k: np.asarray(v) for k, v in inputs.items()}
    sampled = got["L0_rec_sampled_ids"]
    arrays = {
        "ids": np.concatenate([sampled.reshape(SAMPLE_TILES, P).T, got["r_target_movie_id"].reshape(P, TILES),
                               got["r_movie_id"].reshape(P, TILES)], axis=1),
        "sample_row": sampled,
        "front": got["L0_rec_front_emb"],
        "after": np.concatenate([got["L0_rec_after_emb"], got["L0_rec_after_bias"].reshape(VOCAB, 1)], axis=1),
    }
    arrays = {k: np.ascontiguousarray(a) for k, a in arrays.items()}
    args = [nc.dram_tensor(k, a.shape, mybir.dt.from_np(a.dtype), kind="ExternalInput").ap()
            for k, a in arrays.items()]
    out = nc.dram_tensor("out", (BATCH,), mybir.dt.float32, kind="ExternalOutput").ap()
    log_uniform_loss(nc, *args, out)
    return run(nc, [arrays], core_ids=[0]).results[0]["out"]
```

```python
import math

import numpy as np
import concourse.bass as bass
from concourse import mybir
from concourse.alu_op_type import AluOpType as ALU
from contextlib import ExitStack

P = 128
VOCAB = 125000
EMBED = 64
AUG = EMBED + 1
SAMPLES = 1024
BATCH = 2048
SAMPLE_TILES = SAMPLES // P
TILES = BATCH // P
NEG_INF = -1e9
SLOTS = 3
PAIR = 2
WARM_UP = 6
QUARTERS = 4
GROUP = 4
BANK = 512
CORR = SAMPLE_TILES + TILES

SQRT_HALF = 0.70710677
LOG_P = (0.070376836, -0.1151461, 0.116769984)
LOG_Q = (-0.12420141, 0.14249323, -0.16668057)
LOG_R = (0.20000714, -0.24999994, 0.3333333)
LN2_LOW, LN2_HIGH = -0.00021219444, 0.6933594


def log_uniform_loss(nc, ids, sample_row, front, after, out):
    f32, i32 = mybir.dt.float32, mybir.dt.int32
    ACT = mybir.ActivationFunctionType
    AX = mybir.AxisListType
    ctx = ExitStack()
    with ctx:
        def sb(name, shape, dt=f32):
            return ctx.enter_context(nc.sbuf_tensor(name, shape, dt))

        def sem(name):
            return ctx.enter_context(nc.semaphore(name))

        LAB = SAMPLE_TILES
        MOV = SAMPLE_TILES + TILES
        COLS = MOV + TILES
        id_cols = sb("id_cols", [P, COLS], i32)
        wrap = sb("wrap", [P, COLS])
        wrapped = sb("wrapped", [P, COLS])
        rows = sb("rows", [P, COLS], i32)
        label = sb("label", [P, TILES])
        neg_label = sb("neg_label", [P, TILES])
        sample_ids = sb("sample_ids", [P, SAMPLES], i32)
        ident = sb("ident", [P, P])
        big = sb("big", [P, 1])
        ln_big = sb("ln_big", [P, 1])

        w_rows = sb("w_rows", [P, SAMPLE_TILES, AUG])
        x_rows = sb("x_rows", [P, TILES, AUG])
        t_rows = sb("t_rows", [P, TILES, AUG])
        f32r = mybir.dt.float32r
        w_high = sb("w_high", [P, SAMPLE_TILES, 2, EMBED], f32r)
        w_low = sb("w_low", [P, SAMPLE_TILES, 2, EMBED], f32r)
        wT_high = sb("wT_high", [P, SAMPLES], f32r)
        wT_low = sb("wT_low", [P, SAMPLES], f32r)
        x_split = sb("x_split", [P, 2, PAIR, 2, EMBED], f32r)
        xT = sb("xT", [P, 2, PAIR * P], f32r)
        b_cols = sb("b_cols", [P, SAMPLE_TILES])
        b_split = sb("b_split", [P, SAMPLE_TILES, 2], f32r)
        b_parts = sb("b_parts", [P, SAMPLES], f32r)
        ones = sb("ones", [P, P], f32r)
        masks = sb("masks", [P, TILES, SAMPLES])
        prod = sb("prod", [P, TILES, AUG])

        x12 = sb("x12", [P, 2 * CORR])
        expo = sb("expo", [P, 2 * CORR], i32)
        mant_i = sb("mant_i", [P, 2 * CORR], i32)
        small = sb("small", [P, 2 * CORR])
        expf = sb("expf", [P, 2 * CORR])
        mk = sb("mk", [P, 2 * CORR])
        r = sb("r", [P, 2 * CORR])
        r2 = sb("r2", [P, 2 * CORR])
        r3 = sb("r3", [P, 2 * CORR])
        pa = sb("pa", [P, 2 * CORR])
        pq = sb("pq", [P, 2 * CORR])
        pr = sb("pr", [P, 2 * CORR])
        half = sb("half", [P, 2 * CORR])
        logs = sb("logs", [P, 2 * CORR])
        diff = sb("diff", [P, CORR])
        tt = sb("tt", [P, CORR])
        ser = sb("ser", [P, CORR])
        et = sb("et", [P, CORR])
        quot = sb("quot", [P, CORR])
        sel = sb("sel", [P, CORR], i32)
        neg_id = sb("neg_id", [P, CORR])
        log_count = sb("log_count", [P, CORR])

        row_max = sb("row_max", [P, 2, TILES])
        sums = sb("sums", [P, TILES])
        dots = sb("dots", [P, TILES])
        top = sb("top", [P, TILES])
        shifted = sb("shifted", [P, 2, TILES])
        weights = sb("weights", [P, 2, TILES])
        total = sb("total", [P, TILES])
        log_total = sb("log_total", [P, TILES])
        loss = sb("loss", [P, TILES])

        psum = ctx.enter_context(nc.psum_tensor("psum", [P, 8, BANK], f32))

        def logits(t):
            return psum[:, 2 * (t % SLOTS):2 * (t % SLOTS) + 2, :].rearrange("p a n -> p (a n)")

        def x_bank(u):
            return 2 * SLOTS + u % 2

        ids_in = sem("ids_in")
        row_in = sem("row_in")
        rows_ok = sem("rows_ok")
        consts_ok = sem("consts_ok")
        ident_step = sem("ident_step")
        ident_ok = sem("ident_ok")
        labels_ok = sem("labels_ok")
        w_in = [sem(f"w_in{q}") for q in range(QUARTERS)]
        x_in = [sem(f"x_in{k}") for k in range(2)]
        t_in = [sem(f"t_in{k}") for k in range(GROUP)]
        step = sem("step")
        t_ready = sem("t_ready")
        et_ok = sem("et_ok")
        quot_ok = sem("quot_ok")
        log_count_ok = sem("log_count_ok")
        w_high_ok = sem("w_high_ok")
        w_low_ok = sem("w_low_ok")
        w_turned = sem("w_turned")
        wT_high_ok = sem("wT_high_ok")
        wT_low_ok = sem("wT_low_ok")
        b_split_ok = sem("b_split_ok")
        b_turned = sem("b_turned")
        b_parts_ok = sem("b_parts_ok")
        x_high_ok = sem("x_high_ok")
        x_low_ok = sem("x_low_ok")
        x_turned = sem("x_turned")
        xT_ok = sem("xT_ok")
        logits_ok = sem("logits_ok")
        act_mask = sem("act_mask")
        act_square = sem("act_square")
        dve_mask = sem("dve_mask")
        max_ok = sem("max_ok")
        exp_ok = sem("exp_ok")
        dot_ok = sem("dot_ok")
        shifted_ok = sem("shifted_ok")
        weights_ok = sem("weights_ok")
        total_ok = sem("total_ok")
        log_ok = sem("log_ok")
        loss_ok = sem("loss_ok")
        out_ok = sem("out_ok")

        on_act = lambda t: t % 2 == 0
        act_masks = [t for t in range(TILES) if on_act(t)]
        dve_masks = [t for t in range(TILES) if not on_act(t)]

        block = ctx.enter_context(nc.Block())

        @block.sync
        def _(sp):
            sp.dma_start(id_cols[:, :], ids).then_inc(ids_in, 16)
            sp.dma_start(sample_ids[:, :], sample_row.rearrange("(a n) -> a n", a=1).to_broadcast([P, SAMPLES])).then_inc(row_in, 16)
            sp.wait_ge(loss_ok, 1)
            sp.dma_start(out.rearrange("(p t) -> p t", t=TILES), loss[:, :]).then_inc(out_ok, 16)
            sp.wait_ge(out_ok, 16)

        @block.gpsimd
        def _(pool):
            pool.memset(ident[:, :], 0.0).then_inc(ident_step, 1)
            pool.memset(x_rows[:, :, EMBED], 1.0).then_inc(consts_ok, 1)
            pool.memset(ones[:, :].bitcast(f32), 1.0).then_inc(consts_ok, 1)
            pool.memset(b_parts[:, :].bitcast(f32), 0.0).then_inc(consts_ok, 1)
            pool.wait_ge(ident_step, 1)
            pool.affine_select(out=ident[:, :], in_=ident[:, :], compare_op=ALU.not_equal, fill=1.0,
                               base=0, pattern=[[-1, P]], channel_multiplier=1).then_inc(ident_ok, 1)

            def gather(dst, table, col):
                return pool.indirect_dma_start(dst, None, table,
                                               bass.IndirectOffsetOnAxis(ap=rows[:, col:col + 1], axis=0))

            def x_pair(u):
                if u >= 2:
                    pool.wait_ge(x_in[u % 2], 32 * (u // 2))
                for t in (2 * u, 2 * u + 1):
                    gather(x_rows[:, t, 0:EMBED], front, MOV + t).then_inc(x_in[u % 2], 16)

            def true_row(t):
                g, k = divmod(t, GROUP)
                if g:
                    pool.wait_ge(t_in[k], 16 * g)
                gather(t_rows[:, t, :], after, LAB + t).then_inc(t_in[k], 16)

            pool.wait_ge(rows_ok, 1)
            x_pair(0)
            for j in range(SAMPLE_TILES):
                gather(w_rows[:, j, :], after, j).then_inc(w_in[j // 2], 16)
            for u in range(1, TILES // 2):
                x_pair(u)
            for t in range(TILES):
                true_row(t)

        @block.tensor
        def _(pe):
            pe.wait_ge(ident_ok, 1)
            pe.wait_ge(consts_ok, 3)

            def turn_x(u):
                pe.wait_ge(x_low_ok, u + 1)
                if u >= 2:
                    pe.wait_ge(xT_ok, u - 1)
                for i in range(PAIR):
                    m = nc.tensor.transpose(psum[:, x_bank(u), i * P:(i + 1) * P],
                                            x_split[:, u % 2, i].rearrange("p a d -> p (a d)").bitcast(f32), ident[:, :])
                m.then_inc(x_turned, 1)

            def turn_w(q):
                pe.wait_ge(w_low_ok, q + 1)
                for part, src in enumerate((w_high, w_low)):
                    for i in range(2):
                        m = nc.tensor.transpose(psum[:, 2 * q + part, i * P:(i + 1) * P],
                                                src[:, 2 * q + i].rearrange("p a d -> p (a d)").bitcast(f32), ident[:, :])
                m.then_inc(w_turned, 1)

            def turn_b(q):
                pe.wait_ge(b_split_ok, 1 if q < 3 else 2)
                pe.wait_ge(wT_high_ok, q + 1)
                for i in range(2):
                    m = nc.tensor.transpose(psum[0:2, 2 * q, (2 + i) * P:(3 + i) * P],
                                            b_split[:, 2 * q + i, :].bitcast(f32), ident[:, :])
                m.then_inc(b_turned, 1)

            turn_x(0)
            for _ in range(8):
                nc.tensor.matmul(psum[:, 5, :], ones[:, :], b_parts[:, 0:BANK], start=True, stop=True)
            for q in range(QUARTERS - 1):
                turn_w(q)
            pe.wait_ge(xT_ok, 1)
            for q in range(QUARTERS - 1):
                turn_b(q)
            turn_w(3)
            pe.wait_ge(wT_low_ok, 1)
            for _ in range(2):
                nc.tensor.matmul(psum[:, 1, :], wT_high[:, 0:P], wT_high[:, 0:BANK], start=True, stop=True)
            turn_b(3)
            for _ in range(2):
                nc.tensor.matmul(psum[:, 1, :], wT_high[:, 0:P], wT_high[:, 0:BANK], start=True, stop=True)

            def score(t):
                if t >= SLOTS:
                    pe.wait_ge(exp_ok, t - SLOTS + 1)
                for h in range(2):
                    part = slice(h * BANK, (h + 1) * BANK)
                    o = psum[:, 2 * (t % SLOTS) + h, :]
                    x = xT[:, t // 2 % 2, t % 2 * P:(t % 2 + 1) * P]
                    nc.tensor.matmul(o, x, wT_high[:, part], start=True, stop=False)
                    nc.tensor.matmul(o, x, wT_low[:, part], start=False, stop=False)
                    m = nc.tensor.matmul(o, ones[:, :], b_parts[:, part], start=False, stop=True)
                m.then_inc(logits_ok, 1)

            pe.wait_ge(wT_high_ok, QUARTERS)
            pe.wait_ge(wT_low_ok, QUARTERS)
            pe.wait_ge(b_parts_ok, QUARTERS)
            for u in range(TILES // 2):
                pe.wait_ge(xT_ok, u + 1)
                score(2 * u)
                if u + 1 < TILES // 2:
                    turn_x(u + 1)
                score(2 * u + 1)

        @block.scalar
        def _(act):
            nc.scalar.preload_act_table_set("natural_log_exp_and_others")
            made = [0]

            def square(t):
                nc.scalar.activation(masks[:, t, :], sample_ids[:, :], ACT.Square,
                                     bias=neg_label[:, t:t + 1], scale=1.0).then_inc(act_square, 1)

            def hit(t):
                made[0] += 1
                act.wait_ge(act_square, made[0])
                nc.scalar.activation(masks[:, t, :], masks[:, t, :], ACT.Exp, bias=ln_big[:, 0:1],
                                     scale=-256.0).then_inc(act_mask, 1)

            act.wait_ge(row_in, 16)
            act.wait_ge(labels_ok, 1)
            def raise_w(q):
                act.wait_ge(w_in[q], 32)
                j = slice(2 * q, 2 * q + 2)
                nc.scalar.copy(w_high[:, j], w_rows[:, j, 0:EMBED].rearrange("p j (a d) -> p j a d", a=1)
                               .to_broadcast([P, 2, 2, EMBED])).then_inc(w_high_ok, 1)

            def copy_w(q):
                act.wait_ge(w_turned, q + 1)
                c = slice(2 * q * P, (2 * q + 2) * P)
                nc.scalar.copy(wT_high[:, c], psum[:, 2 * q, 0:2 * P]).then_inc(wT_high_ok, 1)

            def copy_b(q):
                act.wait_ge(b_turned, q + 1)
                c = slice(2 * q * P, (2 * q + 2) * P)
                nc.scalar.copy(b_parts[0:2, c], psum[0:2, 2 * q, 2 * P:4 * P]).then_inc(b_parts_ok, 1)

            def raise_x(u):
                act.wait_ge(x_in[u % 2], 32 * (u // 2 + 1))
                if u >= 2:
                    act.wait_ge(x_turned, u - 1)
                nc.scalar.mul(x_split[:, u % 2, :, 0, :], x_rows[:, 2 * u:2 * u + 2, 0:EMBED], -1.0).then_inc(x_high_ok, 1)

            def copy_x(u):
                act.wait_ge(x_turned, u + 1)
                if u >= 2:
                    act.wait_ge(logits_ok, 2 * u - 2)
                nc.scalar.copy(xT[:, u % 2, :], psum[:, x_bank(u), 0:PAIR * P]).then_inc(xT_ok, 1)

            square(0)
            hit(0)
            raise_x(0)
            square(2)
            hit(2)
            raise_w(0)
            copy_x(0)
            square(4)
            act.wait_ge(t_ready, 1)
            nc.scalar.activation(et[:, :], tt[:, :], ACT.Exp, scale=-1.0).then_inc(et_ok, 1)
            raise_w(1)
            act.wait_ge(quot_ok, 1)
            nc.scalar.activation(log_count[:, :], quot[:, :], ACT.Ln).then_inc(log_count_ok, 1)
            hit(4)
            raise_w(2)
            copy_w(0)
            copy_w(1)
            copy_w(2)
            raise_w(3)
            act.wait_ge(consts_ok, 3)
            copy_b(0)
            copy_b(1)
            copy_b(2)
            copy_w(3)
            copy_b(3)
            raise_x(1)
            square(6)
            hit(6)
            todo = [8, 10, 12, 14]

            def exps(t):
                act.wait_ge(max_ok, t + 1)
                nc.scalar.activation(logits(t), logits(t), ACT.Exp, bias=row_max[:, 0, t:t + 1], scale=-1.0,
                                     accum_out=sums[:, t:t + 1]).then_inc(exp_ok, 1)

            for u in range(TILES // 2):
                exps(2 * u)
                if u + 1 < TILES // 2:
                    copy_x(u + 1)
                if u + 2 < TILES // 2:
                    raise_x(u + 2)
                if todo:
                    square(todo[0])
                exps(2 * u + 1)
                if todo:
                    hit(todo.pop(0))
            act.wait_ge(shifted_ok, 1)
            nc.scalar.activation(weights[:, :, :], shifted[:, :, :], ACT.Exp).then_inc(weights_ok, 1)
            act.wait_ge(total_ok, 1)
            nc.scalar.activation(log_total[:, :], total[:, :], ACT.Ln).then_inc(log_ok, 1)

        @block.vector
        def _(dve):
            done = [0]
            V = nc.vector

            def link(ins):
                done[0] += 1
                ins.then_inc(step, 1)
                dve.wait_ge(step, done[0])

            todo = list(dve_masks)

            def make_mask():
                if todo:
                    t = todo.pop(0)
                    V.scalar_tensor_tensor(masks[:, t, :], sample_ids[:, :], label[:, t:t + 1],
                                           big[:, 0:1].to_broadcast([P, SAMPLES]), ALU.is_equal,
                                           ALU.mult).then_inc(dve_mask, 1)

            def lower_w(q):
                dve.wait_ge(w_high_ok, q + 1)
                j = slice(2 * q, 2 * q + 2)
                V.tensor_tensor(w_low[:, j], w_rows[:, j, 0:EMBED].rearrange("p j (a d) -> p j a d", a=1)
                                .to_broadcast([P, 2, 2, EMBED]), w_high[:, j].bitcast(f32),
                                ALU.subtract).then_inc(w_low_ok, 1)

            def copy_w(q):
                dve.wait_ge(w_turned, q + 1)
                c = slice(2 * q * P, (2 * q + 2) * P)
                V.tensor_copy(wT_low[:, c], psum[:, 2 * q + 1, 0:2 * P]).then_inc(wT_low_ok, 1)

            def lower_x(u):
                dve.wait_ge(x_high_ok, u + 1)
                V.scalar_tensor_tensor(x_split[:, u % 2, :, 1, :], x_rows[:, 2 * u:2 * u + 2, 0:EMBED], -1.0,
                                       x_split[:, u % 2, :, 0, :].bitcast(f32), ALU.mult, ALU.subtract).then_inc(x_low_ok, 1)

            dve.wait_ge(ids_in, 16)
            link(V.tensor_scalar(wrap[:, :], id_cols[:, :], 0.0, float(VOCAB), ALU.is_lt, ALU.mult))
            link(V.scalar_tensor_tensor(wrapped[:, :], id_cols[:, :], float(VOCAB - 1), wrap[:, :], ALU.min, ALU.add))
            V.tensor_scalar(rows[:, :], wrapped[:, :], 0.0, None, ALU.max).then_inc(rows_ok, 1)
            V.memset(big[:, :], -NEG_INF)
            V.memset(ln_big[:, :], math.log(-NEG_INF))
            V.tensor_scalar(label[:, :], id_cols[:, LAB:MOV], 1.0, None, ALU.mult)
            link(V.tensor_scalar(neg_label[:, :], id_cols[:, LAB:MOV], -1.0, None, ALU.mult))
            V.tensor_scalar(neg_id[:, :], id_cols[:, 0:CORR], 0.0, 3e38, ALU.min, ALU.mult).then_inc(labels_ok, 1)

            V.tensor_scalar(x12[:, 0:CORR], id_cols[:, 0:CORR], 1.0, None, ALU.add)
            link(V.tensor_scalar(x12[:, CORR:], id_cols[:, 0:CORR], 2.0, None, ALU.add))
            bits = x12[:, :].bitcast(i32)
            V.tensor_scalar(expo[:, :], bits, 23, None, ALU.logical_shift_right)
            link(V.tensor_scalar(mant_i[:, :], bits, 0x7fffff, 0x3f000000, ALU.bitwise_and, ALU.bitwise_or))
            m = mant_i[:, :].bitcast(f32)
            V.tensor_scalar(small[:, :], m, SQRT_HALF, None, ALU.is_lt)
            link(V.scalar_tensor_tensor(mk[:, :], m, SQRT_HALF, m, ALU.is_lt, ALU.mult))
            V.scalar_tensor_tensor(expf[:, :], expo[:, :], 126.0, small[:, :], ALU.subtract, ALU.subtract)
            link(V.scalar_tensor_tensor(r[:, :], m, 1.0, mk[:, :], ALU.subtract, ALU.add))
            V.tensor_scalar(pa[:, :], r[:, :], LOG_P[0], LOG_P[1], ALU.mult, ALU.add)
            V.tensor_scalar(pq[:, :], r[:, :], LOG_Q[0], LOG_Q[1], ALU.mult, ALU.add)
            V.tensor_scalar(pr[:, :], r[:, :], LOG_R[0], LOG_R[1], ALU.mult, ALU.add)
            link(V.tensor_tensor(r2[:, :], r[:, :], r[:, :], ALU.mult))
            V.tensor_tensor(pa[:, :], pa[:, :], r[:, :], ALU.mult)
            V.tensor_tensor(pq[:, :], pq[:, :], r[:, :], ALU.mult)
            V.tensor_tensor(pr[:, :], pr[:, :], r[:, :], ALU.mult)
            V.scalar_tensor_tensor(half[:, :], r2[:, :], -0.5, r[:, :], ALU.mult, ALU.add)
            link(V.tensor_tensor(r3[:, :], r2[:, :], r[:, :], ALU.mult))
            link(V.scalar_tensor_tensor(pa[:, :], pa[:, :], LOG_P[2], r3[:, :], ALU.add, ALU.mult))
            link(V.scalar_tensor_tensor(pa[:, :], pq[:, :], LOG_Q[2], pa[:, :], ALU.add, ALU.add))
            link(V.tensor_tensor(pa[:, :], pa[:, :], r3[:, :], ALU.mult))
            link(V.scalar_tensor_tensor(pa[:, :], pr[:, :], LOG_R[2], pa[:, :], ALU.add, ALU.add))
            link(V.tensor_tensor(pa[:, :], pa[:, :], r3[:, :], ALU.mult))
            link(V.scalar_tensor_tensor(pa[:, :], expf[:, :], LN2_LOW, pa[:, :], ALU.mult, ALU.add))
            link(V.tensor_tensor(half[:, :], half[:, :], pa[:, :], ALU.add))
            link(V.scalar_tensor_tensor(logs[:, :], expf[:, :], LN2_HIGH, half[:, :], ALU.mult, ALU.add))
            link(V.tensor_tensor(diff[:, :], logs[:, CORR:], logs[:, 0:CORR], ALU.subtract))

            lower_x(0)
            log_range = math.log(VOCAB + 1.0)
            c = [SAMPLES / (n * log_range ** n) for n in range(1, 7)]
            link(V.tensor_scalar(tt[:, :], diff[:, :], c[5], c[4], ALU.mult, ALU.add))
            link(V.tensor_tensor(tt[:, :], tt[:, :], diff[:, :], ALU.mult))
            for n in (3, 2, 1):
                link(V.scalar_tensor_tensor(tt[:, :], tt[:, :], c[n], diff[:, :], ALU.add, ALU.mult))
            link(V.scalar_tensor_tensor(tt[:, :], tt[:, :], c[0], diff[:, :], ALU.add, ALU.mult))
            e = [(-1.0) ** n / math.factorial(n + 1) for n in range(8)]
            V.tensor_scalar(sel[:, :], tt[:, :], 0.5, None, ALU.is_lt).then_inc(t_ready, 1)
            link(V.tensor_scalar(ser[:, :], tt[:, :], e[7], e[6], ALU.mult, ALU.add))
            link(V.tensor_tensor(ser[:, :], ser[:, :], tt[:, :], ALU.mult))
            for n in (5, 4, 3, 2, 1, 0):
                link(V.scalar_tensor_tensor(ser[:, :], ser[:, :], e[n], tt[:, :], ALU.add, ALU.mult))
            dve.wait_ge(et_ok, 1)
            link(V.tensor_scalar(quot[:, :], et[:, :], -1.0, 1.0, ALU.mult, ALU.add))
            link(V.copy_predicated(quot[:, :], sel[:, :], ser[:, :]))
            V.tensor_tensor(quot[:, :], quot[:, :], neg_id[:, :], ALU.add).then_inc(quot_ok, 1)

            lower_w(0)
            lower_w(1)

            def split_b(j0, j1):
                j = slice(j0, j1)
                link(V.tensor_tensor(b_cols[:, j], log_count[:, j], w_rows[:, j, EMBED], ALU.subtract))
                link(V.tensor_copy(b_split[:, j, 0], b_cols[:, j]))
                V.tensor_tensor(b_split[:, j, 1], b_cols[:, j], b_split[:, j, 0].bitcast(f32), ALU.subtract).then_inc(b_split_ok, 1)

            lower_w(2)
            dve.wait_ge(log_count_ok, 1)
            for q in range(3):
                dve.wait_ge(w_in[q], 32)
            split_b(0, 6)
            copy_w(0)
            copy_w(1)
            copy_w(2)
            dve.wait_ge(w_in[3], 32)
            split_b(6, 8)
            lower_w(3)
            dve.wait_ge(row_in, 16)
            make_mask()
            copy_w(3)
            lower_x(1)
            make_mask()

            def top_logit(t):
                dve.wait_ge(logits_ok, t + 1)
                if on_act(t):
                    dve.wait_ge(act_mask, act_masks.index(t) + 1)
                else:
                    dve.wait_ge(dve_mask, dve_masks.index(t) + 1)
                V.tensor_tensor_reduce(out=logits(t), in0=logits(t), in1=masks[:, t, :],
                                       scale=1.0, scalar=3e38, op0=ALU.add, op1=ALU.min,
                                       accum_out=row_max[:, 0, t:t + 1]).then_inc(max_ok, 1)

            def dot(t):
                g, k = divmod(t, GROUP)
                dve.wait_ge(x_in[t // 2 % 2], 32 * (t // 4 + 1))
                dve.wait_ge(t_in[k], 16 * (g + 1))
                V.tensor_tensor_reduce(out=prod[:, t, :], in0=x_rows[:, t, :], in1=t_rows[:, t, :],
                                       scale=1.0, scalar=0.0, op0=ALU.mult, op1=ALU.add,
                                       accum_out=dots[:, t:t + 1]).then_inc(dot_ok, 1)

            dots_at = {8: 1, 9: 2, 10: 2, 11: 2, 12: 2, 13: 2, 14: 2, 15: 3}
            dots_done = 0
            dve.wait_ge(consts_ok, 3)
            for t in range(TILES):
                top_logit(t)
                if t % 2 and t // 2 + 2 < TILES // 2:
                    lower_x(t // 2 + 2)
                if t % 2 == 0:
                    make_mask()
                for _ in range(dots_at.get(t, 0)):
                    dot(dots_done)
                    dots_done += 1
            dve.wait_ge(dot_ok, TILES)
            link(V.tensor_tensor(row_max[:, 1, :], log_count[:, SAMPLE_TILES:], dots[:, :], ALU.subtract))
            link(V.tensor_tensor(top[:, :], row_max[:, 0, :], row_max[:, 1, :], ALU.min))
            V.tensor_tensor(shifted[:, 0, :], top[:, :], row_max[:, 0, :], ALU.subtract)
            V.tensor_tensor(shifted[:, 1, :], top[:, :], row_max[:, 1, :], ALU.subtract).then_inc(shifted_ok, 1)
            dve.wait_ge(weights_ok, 1)
            dve.wait_ge(exp_ok, TILES)
            link(V.tensor_tensor(total[:, :], sums[:, :], weights[:, 0, :], ALU.mult))
            V.tensor_tensor(total[:, :], total[:, :], weights[:, 1, :], ALU.add).then_inc(total_ok, 1)
            dve.wait_ge(log_ok, 1)
            V.tensor_tensor(loss[:, :], log_total[:, :], shifted[:, 1, :], ALU.subtract).then_inc(loss_ok, 1)


def kernel(**inputs):
    import concourse.bacc as bacc
    from concourse.bass_utils import run_bass_kernel_spmd as run

    nc = bacc.Bacc("TRN2", target_bir_lowering=False, num_devices=1)
    got = {k: np.asarray(v) for k, v in inputs.items()}
    sampled = got["L0_rec_sampled_ids"]
    arrays = {
        "ids": np.concatenate([sampled.reshape(SAMPLE_TILES, P).T, got["r_target_movie_id"].reshape(P, TILES),
                               got["r_movie_id"].reshape(P, TILES)], axis=1),
        "sample_row": sampled,
        "front": got["L0_rec_front_emb"],
        "after": np.concatenate([got["L0_rec_after_emb"], got["L0_rec_after_bias"].reshape(VOCAB, 1)], axis=1),
    }
    arrays = {k: np.ascontiguousarray(a) for k, a in arrays.items()}
    args = [nc.dram_tensor(k, a.shape, mybir.dt.from_np(a.dtype), kind="ExternalInput").ap()
            for k, a in arrays.items()]
    out = nc.dram_tensor("out", (BATCH,), mybir.dt.float32, kind="ExternalOutput").ap()
    log_uniform_loss(nc, *args, out)
    return run(nc, [arrays], core_ids=[0]).results[0]["out"]
```

```python
import math
from contextlib import ExitStack

import numpy as np
import concourse.bass as bass
from concourse import mybir
from concourse.alu_op_type import AluOpType as ALU

P = 128
VOCAB = 125000
EMBED = 64
AUG = EMBED + 1
SAMPLES = 1024
BATCH = 2048
SAMPLE_TILES = SAMPLES // P
TILES = BATCH // P
NEG_INF = -1e9
BANK = 512
SLOTS = 3
QUARTERS = 4
T_SEMS = 4
CORR = SAMPLE_TILES + TILES
X_GROUPS = [(0, 1), (1, 2)] + [(t, t + 2) for t in range(2, TILES, 2)]
ACT_MASKS = (0, 2, 4, 6, 8, 10, 12, 13, 15)

SQRT_HALF = 0.70710677
LOG_P = (0.070376836, -0.1151461, 0.116769984)
LOG_Q = (-0.12420141, 0.14249323, -0.16668057)
LOG_R = (0.20000714, -0.24999994, 0.3333333)
LN2_LOW, LN2_HIGH = -0.00021219444, 0.6933594


def log_uniform_loss(nc, ids, sample_row, front, after, out):
    f32, f32r, i32 = mybir.dt.float32, mybir.dt.float32r, mybir.dt.int32
    ACT = mybir.ActivationFunctionType
    ctx = ExitStack()
    with ctx:
        def sb(name, shape, dt=f32):
            return ctx.enter_context(nc.sbuf_tensor(name, shape, dt))

        def sem(name):
            return ctx.enter_context(nc.semaphore(name))

        LAB = SAMPLE_TILES
        MOV = SAMPLE_TILES + TILES
        COLS = MOV + TILES
        id_cols = sb("id_cols", [P, COLS], i32)
        wrap = sb("wrap", [P, COLS])
        wrapped = sb("wrapped", [P, COLS])
        rows = sb("rows", [P, COLS], i32)
        label = sb("label", [P, TILES])
        neg_label = sb("neg_label", [P, TILES])
        sample_ids = sb("sample_ids", [P, SAMPLES], i32)
        ident = sb("ident", [P, P])
        big = sb("big", [P, 1])
        ln_big = sb("ln_big", [P, 1])

        w_rows = sb("w_rows", [P, SAMPLE_TILES, AUG])
        x_rows = sb("x_rows", [P, TILES, AUG])
        t_rows = sb("t_rows", [P, TILES, AUG])
        wT_high = sb("wT_high", [P, SAMPLES], f32r)
        wT_low = sb("wT_low", [P, SAMPLES], f32r)
        xT = sb("xT", [P, BATCH], f32r)
        b_cols = sb("b_cols", [P, SAMPLE_TILES])
        b_split = sb("b_split", [P, SAMPLE_TILES, 2], f32r)
        b_parts = sb("b_parts", [P, SAMPLES], f32r)
        ones = sb("ones", [P, P], f32r)
        masks = sb("masks", [P, TILES, SAMPLES])
        prod = sb("prod", [P, TILES, AUG])

        arg = sb("arg", [P, 2 * CORR])
        expo_i = sb("expo_i", [P, 2 * CORR], i32)
        mant_i = sb("mant_i", [P, 2 * CORR], i32)
        small = sb("small", [P, 2 * CORR])
        expo = sb("expo", [P, 2 * CORR])
        mant_small = sb("mant_small", [P, 2 * CORR])
        r = sb("r", [P, 2 * CORR])
        r2 = sb("r2", [P, 2 * CORR])
        r3 = sb("r3", [P, 2 * CORR])
        poly = sb("poly", [P, 2 * CORR])
        poly_q = sb("poly_q", [P, 2 * CORR])
        poly_r = sb("poly_r", [P, 2 * CORR])
        half = sb("half", [P, 2 * CORR])
        logs = sb("logs", [P, 2 * CORR])
        diff = sb("diff", [P, CORR])
        tries = sb("tries", [P, CORR])
        series = sb("series", [P, CORR])
        exp_tries = sb("exp_tries", [P, CORR])
        is_small = sb("is_small", [P, CORR], i32)
        count = sb("count", [P, CORR])
        below = sb("below", [P, CORR])
        log_count = sb("log_count", [P, CORR])

        lowest = sb("lowest", [P, 2, TILES])
        sums = sb("sums", [P, TILES])
        dots = sb("dots", [P, TILES])
        floor = sb("floor", [P, TILES])
        shifted = sb("shifted", [P, 2, TILES])
        weights = sb("weights", [P, 2, TILES])
        total = sb("total", [P, TILES])
        log_total = sb("log_total", [P, TILES])
        loss = sb("loss", [P, TILES])

        psum = ctx.enter_context(nc.psum_tensor("psum", [P, 8, BANK], f32))

        def logits(t):
            return psum[:, 2 * (t % SLOTS):2 * (t % SLOTS) + 2, :].rearrange("p a n -> p (a n)")

        def x_bank(g):
            return 2 * SLOTS + g % 2

        def x_arrived(g):
            return sum(16 * (b - a) for a, b in X_GROUPS[g % 2:g + 1:2])

        def x_cols(g):
            a, b = X_GROUPS[g]
            return slice(a * P, b * P)

        def group_of(t):
            return t if t < 2 else t // 2 + 1

        def w_cols(q):
            return slice(2 * q * P, (2 * q + 2) * P)

        ids_in = sem("ids_in")
        row_in = sem("row_in")
        rows_ok = sem("rows_ok")
        consts_ok = sem("consts_ok")
        ident_zero = sem("ident_zero")
        ident_ok = sem("ident_ok")
        labels_ok = sem("labels_ok")
        w_in = [sem(f"w_in{q}") for q in range(QUARTERS)]
        x_in = [sem(f"x_in{k}") for k in range(2)]
        t_in = [sem(f"t_in{k}") for k in range(T_SEMS)]
        step = sem("step")
        tries_ok = sem("tries_ok")
        exp_tries_ok = sem("exp_tries_ok")
        count_ok = sem("count_ok")
        log_count_ok = sem("log_count_ok")
        w_turned = sem("w_turned")
        wT_high_ok = sem("wT_high_ok")
        wT_low_ok = sem("wT_low_ok")
        b_split_ok = sem("b_split_ok")
        b_turned = sem("b_turned")
        b_parts_ok = sem("b_parts_ok")
        x_turned = sem("x_turned")
        x_high_ok = sem("x_high_ok")
        xT_ok = sem("xT_ok")
        logits_ok = sem("logits_ok")
        act_square = sem("act_square")
        act_mask = sem("act_mask")
        dve_mask = sem("dve_mask")
        lowest_ok = sem("lowest_ok")
        exp_ok = sem("exp_ok")
        dot_ok = sem("dot_ok")
        shifted_ok = sem("shifted_ok")
        weights_ok = sem("weights_ok")
        total_ok = sem("total_ok")
        log_ok = sem("log_ok")
        loss_ok = sem("loss_ok")
        out_ok = sem("out_ok")

        DVE_MASKS = [t for t in range(TILES) if t not in ACT_MASKS]

        block = ctx.enter_context(nc.Block())

        @block.sync
        def _(sp):
            sp.dma_start(id_cols[:, :], ids).then_inc(ids_in, 16)
            sp.dma_start(sample_ids[:, :], sample_row.rearrange("(a n) -> a n", a=1).to_broadcast([P, SAMPLES])
                         ).then_inc(row_in, 16)
            sp.wait_ge(loss_ok, 1)
            sp.dma_start(out.rearrange("(p t) -> p t", t=TILES), loss[:, :]).then_inc(out_ok, 16)
            sp.wait_ge(out_ok, 16)

        @block.gpsimd
        def _(pool):
            pool.memset(ident[:, :], 0.0).then_inc(ident_zero, 1)
            pool.memset(x_rows[:, :, EMBED], 1.0).then_inc(consts_ok, 1)
            pool.memset(ones[:, :].bitcast(f32), 1.0).then_inc(consts_ok, 1)
            pool.memset(b_parts[:, :].bitcast(f32), 0.0).then_inc(consts_ok, 1)
            pool.wait_ge(ident_zero, 1)
            pool.affine_select(out=ident[:, :], in_=ident[:, :], compare_op=ALU.not_equal, fill=1.0,
                               base=0, pattern=[[-1, P]], channel_multiplier=1).then_inc(ident_ok, 1)

            def gather(dst, table, col):
                return pool.indirect_dma_start(dst, None, table,
                                               bass.IndirectOffsetOnAxis(ap=rows[:, col:col + 1], axis=0))

            pool.wait_ge(rows_ok, 1)
            for j in range(SAMPLE_TILES):
                gather(w_rows[:, j, :], after, j).then_inc(w_in[j // 2], 16)
            for g in range(len(X_GROUPS)):
                if g >= 2:
                    pool.wait_ge(x_in[g % 2], x_arrived(g - 2))
                for t in range(*X_GROUPS[g]):
                    gather(x_rows[:, t, 0:EMBED], front, MOV + t).then_inc(x_in[g % 2], 16)
            for t in range(TILES):
                if t >= T_SEMS:
                    pool.wait_ge(t_in[t % T_SEMS], 16 * (t // T_SEMS))
                gather(t_rows[:, t, :], after, LAB + t).then_inc(t_in[t % T_SEMS], 16)

        @block.tensor
        def _(pe):
            pe.wait_ge(ident_ok, 1)
            pe.wait_ge(consts_ok, 3)

            def turn_w(q):
                pe.wait_ge(w_in[q], 32)
                for i in range(2):
                    m = nc.tensor.transpose(psum[0:EMBED, q, i * P:(i + 1) * P], w_rows[:, 2 * q + i, 0:EMBED],
                                            ident[:, :])
                m.then_inc(w_turned, 1)

            def turn_b(h):
                for i in range(4):
                    m = nc.tensor.transpose(psum[0:2, 4 + h, i * P:(i + 1) * P],
                                            b_split[:, 4 * h + i, :].bitcast(f32), ident[:, :])
                m.then_inc(b_turned, 1)

            def turn_x(g):
                pe.wait_ge(x_in[g % 2], x_arrived(g))
                if g >= 2:
                    pe.wait_ge(xT_ok, g - 1)
                for i, t in enumerate(range(*X_GROUPS[g])):
                    m = nc.tensor.transpose(psum[0:EMBED, x_bank(g), i * P:(i + 1) * P], x_rows[:, t, 0:EMBED],
                                            ident[:, :])
                m.then_inc(x_turned, 1)

            def keep_busy(n):
                for _ in range(n):
                    nc.tensor.matmul(psum[:, 7, :], ones[:, :], ones[:, 0:1].to_broadcast([P, BANK]),
                                     start=True, stop=True)

            for q in range(QUARTERS):
                turn_w(q)
                keep_busy((2, 4, 4, 0)[q])
            pe.wait_ge(b_split_ok, 1)
            turn_b(0)
            turn_b(1)
            keep_busy(1)
            turn_x(0)
            turn_x(1)

            def score(t):
                if t >= SLOTS:
                    pe.wait_ge(exp_ok, t - SLOTS + 1)
                x = xT[:, t * P:(t + 1) * P]
                for h in range(2):
                    part = slice(h * BANK, (h + 1) * BANK)
                    o = psum[:, 2 * (t % SLOTS) + h, :]
                    nc.tensor.matmul(o, x, wT_high[:, part], start=True, stop=False)
                    nc.tensor.matmul(o, x, wT_low[:, part], start=False, stop=False)
                    m = nc.tensor.matmul(o, ones[:, :], b_parts[:, part], start=False, stop=True)
                m.then_inc(logits_ok, 1)

            pe.wait_ge(wT_low_ok, QUARTERS)
            pe.wait_ge(b_parts_ok, 2)
            for t in range(TILES):
                if t % 2 == 0 and 2 <= t < TILES - 2:
                    turn_x(group_of(t + 2))
                pe.wait_ge(xT_ok, group_of(t) + 1)
                score(t)
                if t == 0:
                    turn_x(group_of(2))

        @block.scalar
        def _(act):
            nc.scalar.preload_act_table_set("natural_log_exp_and_others")

            def square(t):
                nc.scalar.activation(masks[:, t, :], sample_ids[:, :], ACT.Square,
                                     bias=neg_label[:, t:t + 1], scale=1.0).then_inc(act_square, 1)

            def hit(t):
                act.wait_ge(act_square, ACT_MASKS.index(t) + 1)
                nc.scalar.activation(masks[:, t, :], masks[:, t, :], ACT.Exp, bias=ln_big[:, 0:1],
                                     scale=-256.0).then_inc(act_mask, 1)

            def raise_w(q):
                act.wait_ge(w_turned, q + 1)
                nc.scalar.copy(wT_high[0:EMBED, w_cols(q)], psum[0:EMBED, q, 0:2 * P])
                nc.scalar.copy(wT_high[EMBED:, w_cols(q)], psum[0:EMBED, q, 0:2 * P]).then_inc(wT_high_ok, 1)

            def copy_b(h):
                act.wait_ge(b_turned, h + 1)
                nc.scalar.copy(b_parts[0:2, h * BANK:(h + 1) * BANK], psum[0:2, 4 + h, :]).then_inc(b_parts_ok, 1)

            def raise_x(g):
                act.wait_ge(x_turned, g + 1)
                n = x_cols(g).stop - x_cols(g).start
                nc.scalar.mul(xT[0:EMBED, x_cols(g)], psum[0:EMBED, x_bank(g), 0:n], -1.0).then_inc(x_high_ok, 1)

            def exps(t):
                act.wait_ge(lowest_ok, t + 1)
                nc.scalar.activation(logits(t), logits(t), ACT.Exp, bias=lowest[:, 0, t:t + 1], scale=-1.0,
                                     accum_out=sums[:, t:t + 1]).then_inc(exp_ok, 1)

            act.wait_ge(consts_ok, 3)
            act.wait_ge(row_in, 16)
            act.wait_ge(labels_ok, 1)
            square(0)
            hit(0)
            square(2)
            raise_w(0)
            hit(2)
            act.wait_ge(tries_ok, 1)
            nc.scalar.activation(exp_tries[:, :], tries[:, :], ACT.Exp, scale=-1.0).then_inc(exp_tries_ok, 1)
            raise_w(1)
            square(4)
            raise_w(2)
            act.wait_ge(count_ok, 1)
            nc.scalar.activation(log_count[:, :], count[:, :], ACT.Ln).then_inc(log_count_ok, 1)
            hit(4)
            raise_w(3)
            copy_b(0)
            copy_b(1)
            raise_x(0)
            raise_x(1)
            square(6)
            hit(6)
            raise_x(2)
            square(8)

            between = {0: (hit, 8), 1: (hit, 10), 2: (square, 12), 3: (square, 13), 4: (hit, 13),
                       5: (square, 15), 6: (hit, 15)}
            behind = {0: (square, 10), 2: (hit, 12)}
            for u in range(TILES // 2):
                exps(2 * u)
                if 2 * u + 4 < TILES:
                    raise_x(group_of(2 * u + 4))
                if u in between:
                    make, t = between[u]
                    make(t)
                exps(2 * u + 1)
                if u in behind:
                    make, t = behind[u]
                    make(t)

            act.wait_ge(shifted_ok, 1)
            nc.scalar.activation(weights[:, :, :], shifted[:, :, :], ACT.Exp).then_inc(weights_ok, 1)
            act.wait_ge(total_ok, 1)
            nc.scalar.activation(log_total[:, :], total[:, :], ACT.Ln).then_inc(log_ok, 1)

        @block.vector
        def _(dve):
            V = nc.vector
            linked = [0]

            def link(ins):
                linked[0] += 1
                ins.then_inc(step, 1)
                dve.wait_ge(step, linked[0])

            def make_mask(t):
                V.scalar_tensor_tensor(masks[:, t, :], sample_ids[:, :], label[:, t:t + 1],
                                       big[:, 0:1].to_broadcast([P, SAMPLES]), ALU.is_equal,
                                       ALU.mult).then_inc(dve_mask, 1)

            def lower_w(q):
                dve.wait_ge(wT_high_ok, q + 1)
                for half_rows in (slice(0, EMBED), slice(EMBED, P)):
                    m = V.tensor_tensor(wT_low[half_rows, w_cols(q)], psum[0:EMBED, q, 0:2 * P],
                                        wT_high[0:EMBED, w_cols(q)].bitcast(f32), ALU.subtract)
                m.then_inc(wT_low_ok, 1)

            def lower_x(g):
                dve.wait_ge(x_high_ok, g + 1)
                n = x_cols(g).stop - x_cols(g).start
                V.scalar_tensor_tensor(xT[EMBED:, x_cols(g)], psum[0:EMBED, x_bank(g), 0:n], -1.0,
                                       xT[0:EMBED, x_cols(g)].bitcast(f32), ALU.mult, ALU.subtract).then_inc(xT_ok, 1)

            dve.wait_ge(ids_in, 16)
            V.tensor_scalar(wrap[:, :], id_cols[:, :], 0.0, float(VOCAB), ALU.is_lt, ALU.mult)
            link(V.tensor_scalar(wrapped[:, :], id_cols[:, :], float(-VOCAB), float(VOCAB - 1), ALU.max, ALU.min))
            V.tensor_tensor(rows[:, :], wrapped[:, :], wrap[:, :], ALU.add).then_inc(rows_ok, 1)
            V.memset(big[:, :], -NEG_INF)
            V.memset(ln_big[:, :], math.log(-NEG_INF))
            V.tensor_scalar(label[:, :], id_cols[:, LAB:MOV], 1.0, None, ALU.mult)
            V.tensor_scalar(neg_label[:, :], id_cols[:, LAB:MOV], -1.0, None, ALU.mult).then_inc(labels_ok, 1)
            V.tensor_scalar(below[:, :], id_cols[:, 0:CORR], 0.0, 3e38, ALU.min, ALU.mult)

            V.tensor_scalar(arg[:, 0:CORR], id_cols[:, 0:CORR], 1.0, None, ALU.add)
            link(V.tensor_scalar(arg[:, CORR:], id_cols[:, 0:CORR], 2.0, None, ALU.add))
            bits = arg[:, :].bitcast(i32)
            V.tensor_scalar(expo_i[:, :], bits, 23, None, ALU.logical_shift_right)
            link(V.tensor_scalar(mant_i[:, :], bits, 0x7fffff, 0x3f000000, ALU.bitwise_and, ALU.bitwise_or))
            m = mant_i[:, :].bitcast(f32)
            V.tensor_scalar(small[:, :], m, SQRT_HALF, None, ALU.is_lt)
            link(V.scalar_tensor_tensor(mant_small[:, :], m, SQRT_HALF, m, ALU.is_lt, ALU.mult))
            V.scalar_tensor_tensor(expo[:, :], expo_i[:, :], 126.0, small[:, :], ALU.subtract, ALU.subtract)
            link(V.scalar_tensor_tensor(r[:, :], m, 1.0, mant_small[:, :], ALU.subtract, ALU.add))
            V.tensor_scalar(poly[:, :], r[:, :], LOG_P[0], LOG_P[1], ALU.mult, ALU.add)
            V.tensor_scalar(poly_q[:, :], r[:, :], LOG_Q[0], LOG_Q[1], ALU.mult, ALU.add)
            V.tensor_scalar(poly_r[:, :], r[:, :], LOG_R[0], LOG_R[1], ALU.mult, ALU.add)
            link(V.tensor_tensor(r2[:, :], r[:, :], r[:, :], ALU.mult))
            V.tensor_tensor(poly[:, :], poly[:, :], r[:, :], ALU.mult)
            V.tensor_tensor(poly_q[:, :], poly_q[:, :], r[:, :], ALU.mult)
            V.tensor_tensor(poly_r[:, :], poly_r[:, :], r[:, :], ALU.mult)
            V.scalar_tensor_tensor(half[:, :], r2[:, :], -0.5, r[:, :], ALU.mult, ALU.add)
            link(V.tensor_tensor(r3[:, :], r2[:, :], r[:, :], ALU.mult))
            link(V.scalar_tensor_tensor(poly[:, :], poly[:, :], LOG_P[2], r3[:, :], ALU.add, ALU.mult))
            link(V.scalar_tensor_tensor(poly[:, :], poly_q[:, :], LOG_Q[2], poly[:, :], ALU.add, ALU.add))
            link(V.tensor_tensor(poly[:, :], poly[:, :], r3[:, :], ALU.mult))
            link(V.scalar_tensor_tensor(poly[:, :], poly_r[:, :], LOG_R[2], poly[:, :], ALU.add, ALU.add))
            link(V.tensor_tensor(poly[:, :], poly[:, :], r3[:, :], ALU.mult))
            link(V.scalar_tensor_tensor(poly[:, :], expo[:, :], LN2_LOW, poly[:, :], ALU.mult, ALU.add))
            link(V.tensor_tensor(half[:, :], half[:, :], poly[:, :], ALU.add))
            link(V.scalar_tensor_tensor(logs[:, :], expo[:, :], LN2_HIGH, half[:, :], ALU.mult, ALU.add))
            link(V.tensor_tensor(diff[:, :], logs[:, CORR:], logs[:, 0:CORR], ALU.subtract))

            log_range = math.log(VOCAB + 1.0)
            c = [SAMPLES / (n * log_range ** n) for n in range(1, 6)]
            link(V.tensor_scalar(tries[:, :], diff[:, :], c[4], c[3], ALU.mult, ALU.add))
            link(V.tensor_tensor(tries[:, :], tries[:, :], diff[:, :], ALU.mult))
            for n in (2, 1, 0):
                link(V.scalar_tensor_tensor(tries[:, :], tries[:, :], c[n], diff[:, :], ALU.add, ALU.mult))
            e = [(-1.0) ** n / math.factorial(n + 1) for n in range(7)]
            V.tensor_scalar(is_small[:, :], tries[:, :], 0.5, None, ALU.is_lt).then_inc(tries_ok, 1)
            link(V.tensor_scalar(series[:, :], tries[:, :], e[6], e[5], ALU.mult, ALU.add))
            link(V.tensor_tensor(series[:, :], series[:, :], tries[:, :], ALU.mult))
            for n in (4, 3, 2, 1, 0):
                link(V.scalar_tensor_tensor(series[:, :], series[:, :], e[n], tries[:, :], ALU.add, ALU.mult))
            dve.wait_ge(exp_tries_ok, 1)
            link(V.tensor_scalar(count[:, :], exp_tries[:, :], -1.0, 1.0, ALU.mult, ALU.add))
            link(V.copy_predicated(count[:, :], is_small[:, :], series[:, :]))
            V.tensor_tensor(count[:, :], count[:, :], below[:, :], ALU.add).then_inc(count_ok, 1)

            lower_w(0)
            lower_w(1)
            lower_w(2)
            for q in range(QUARTERS):
                dve.wait_ge(w_in[q], 32)
            dve.wait_ge(log_count_ok, 1)
            link(V.tensor_tensor(b_cols[:, :], log_count[:, 0:SAMPLE_TILES], w_rows[:, :, EMBED], ALU.subtract))
            link(V.tensor_copy(b_split[:, :, 0], b_cols[:, :]))
            V.tensor_tensor(b_split[:, :, 1], b_cols[:, :], b_split[:, :, 0].bitcast(f32),
                            ALU.subtract).then_inc(b_split_ok, 1)
            dve.wait_ge(row_in, 16)
            make_mask(DVE_MASKS[0])
            lower_w(3)
            lower_x(0)
            lower_x(1)
            make_mask(DVE_MASKS[1])

            def mask_and_reduce(t):
                dve.wait_ge(logits_ok, t + 1)
                if t in ACT_MASKS:
                    dve.wait_ge(act_mask, ACT_MASKS.index(t) + 1)
                else:
                    dve.wait_ge(dve_mask, DVE_MASKS.index(t) + 1)
                V.tensor_tensor_reduce(out=logits(t), in0=logits(t), in1=masks[:, t, :],
                                       scale=1.0, scalar=3e38, op0=ALU.add, op1=ALU.min,
                                       accum_out=lowest[:, 0, t:t + 1]).then_inc(lowest_ok, 1)

            def dot(t):
                g = group_of(t)
                dve.wait_ge(x_in[g % 2], x_arrived(g))
                dve.wait_ge(t_in[t % T_SEMS], 16 * (t // T_SEMS + 1))
                V.tensor_tensor_reduce(out=prod[:, t, :], in0=x_rows[:, t, :], in1=t_rows[:, t, :],
                                       scale=1.0, scalar=0.0, op0=ALU.mult, op1=ALU.add,
                                       accum_out=dots[:, t:t + 1]).then_inc(dot_ok, 1)

            dots_behind = {8: 1, 9: 2, 10: 2, 11: 2, 12: 2, 13: 2, 14: 4, 15: 1}
            dots_done = 0
            dve.wait_ge(consts_ok, 3)
            for t in range(TILES):
                mask_and_reduce(t)
                if t == 0:
                    lower_x(group_of(2))
                if t % 2 and t + 3 < TILES:
                    lower_x(group_of(t + 3))
                if t % 2 == 0 and t // 2 + 2 < len(DVE_MASKS):
                    make_mask(DVE_MASKS[t // 2 + 2])
                for _ in range(dots_behind.get(t, 0)):
                    dot(dots_done)
                    dots_done += 1

            dve.wait_ge(dot_ok, TILES)
            link(V.tensor_tensor(lowest[:, 1, :], log_count[:, SAMPLE_TILES:], dots[:, :], ALU.subtract))
            link(V.tensor_tensor(floor[:, :], lowest[:, 0, :], lowest[:, 1, :], ALU.min))
            V.tensor_tensor(shifted[:, 0, :], floor[:, :], lowest[:, 0, :], ALU.subtract)
            V.tensor_tensor(shifted[:, 1, :], floor[:, :], lowest[:, 1, :], ALU.subtract).then_inc(shifted_ok, 1)
            dve.wait_ge(weights_ok, 1)
            dve.wait_ge(exp_ok, TILES)
            link(V.tensor_tensor(total[:, :], sums[:, :], weights[:, 0, :], ALU.mult))
            V.tensor_tensor(total[:, :], total[:, :], weights[:, 1, :], ALU.add).then_inc(total_ok, 1)
            dve.wait_ge(log_ok, 1)
            V.tensor_tensor(loss[:, :], log_total[:, :], shifted[:, 1, :], ALU.subtract).then_inc(loss_ok, 1)


def kernel(**inputs):
    import concourse.bacc as bacc
    from concourse.bass_utils import run_bass_kernel_spmd as run

    nc = bacc.Bacc("TRN2", target_bir_lowering=False, num_devices=1)
    got = {k: np.asarray(v) for k, v in inputs.items()}
    sampled = got["L0_rec_sampled_ids"]
    arrays = {
        "ids": np.concatenate([sampled.reshape(SAMPLE_TILES, P).T, got["r_target_movie_id"].reshape(P, TILES),
                               got["r_movie_id"].reshape(P, TILES)], axis=1),
        "sample_row": sampled,
        "front": got["L0_rec_front_emb"],
        "after": np.concatenate([got["L0_rec_after_emb"], got["L0_rec_after_bias"].reshape(VOCAB, 1)], axis=1),
    }
    arrays = {k: np.ascontiguousarray(a) for k, a in arrays.items()}
    args = [nc.dram_tensor(k, a.shape, mybir.dt.from_np(a.dtype), kind="ExternalInput").ap()
            for k, a in arrays.items()]
    out = nc.dram_tensor("out", (BATCH,), mybir.dt.float32, kind="ExternalOutput").ap()
    log_uniform_loss(nc, *args, out)
    return run(nc, [arrays], core_ids=[0]).results[0]["out"]
```
